# Optimizing a Trainium2 kernel written in Bass

```python
import numpy as np
import jax
import jax.numpy as jnp

def _softmax(x, axis=-1):
    return jax.nn.softmax(x, axis=axis)

def _gelu(x):
    return jax.nn.gelu(x, approximate=True)

def _silu(x):
    return jax.nn.silu(x)

def _sigmoid(x):
    return jax.nn.sigmoid(x)

def _layernorm(x, axis=-1, eps=1e-05):
    m = jnp.mean(x, axis=axis, keepdims=True)
    v = jnp.var(x, axis=axis, keepdims=True)
    return (x - m) / jnp.sqrt(v + eps)

def _scatter_add(tgt, idx, src, axis=0):
    return tgt.at[idx].add(src)

def _segment_sum(src, seg, n):
    return jax.ops.segment_sum(src, seg, n)
kernel_name = 'mk_adj_resnorm_d1_adj_r2_546442'

def setup_inputs(seed: int=0):
    np.random.seed(seed)
    _w = jnp.asarray

    def _rec_inputs():
        import jax
        import jax.numpy as jnp
        _gk = jax.random.key(seed)
        x = 7.22e-05 + 1 * jax.random.normal(jax.random.fold_in(_gk, 1), (16, 512, 256), jnp.float32)
        _w = (1.0 + jnp.arange(512, dtype=jnp.float32)) ** (-0.5)
        _w = _w / _w.mean()
        _pij = jnp.clip(0.0078125 * _w[:, None] * _w[None, :], 0.0, 1.0)
        _a = jax.random.uniform(jax.random.fold_in(_gk, 2), (512, 512)) < _pij
        _a = jnp.logical_or(_a, jnp.swapaxes(_a, -1, -2))
        _a = jnp.logical_or(_a, jnp.eye(512, dtype=bool))
        _af = _a.astype(jnp.float32)
        _af = _af * jax.random.uniform(jax.random.fold_in(_gk, 3), (512, 512), jnp.float32, 0.05, 0.00390622)
        adj = _af
        return (x, adj)
    x, adj = _rec_inputs()

    def _L0_gnn_setup():
        import jax, jax.numpy as jnp
        import numpy as np
        B, N, D, T = (64, 128, 256, 3)

        def _lin(v, W, b):
            return jnp.einsum('...i,oi->...o', v, W) + b
        key = jax.random.key(seed)
        ks = jax.random.split(key, 12)
        s2 = 1.0 / np.sqrt(2 * D)
        s1 = 1.0 / np.sqrt(D)
        return {'x': jax.random.normal(ks[0], (B, N, D), jnp.float32), 'in_mat': jax.random.uniform(ks[1], (N, N), jnp.float32) / N, 'out_mat': jax.random.uniform(ks[2], (N, N), jnp.float32) / N, 'w3_w': jax.random.normal(ks[3], (D, 2 * D), jnp.float32) * s2, 'w3_b': jnp.zeros((D,), jnp.float32), 'u3_w': jax.random.normal(ks[4], (D, D), jnp.float32) * s1, 'u3_b': jnp.zeros((D,), jnp.float32), 'w4_w': jax.random.normal(ks[5], (D, 2 * D), jnp.float32) * s2, 'w4_b': jnp.zeros((D,), jnp.float32), 'w5_w': jax.random.normal(ks[6], (D, 2 * D), jnp.float32) * s2, 'w5_b': jnp.zeros((D,), jnp.float32), 'u5_w': jax.random.normal(ks[7], (D, D), jnp.float32) * s1, 'u5_b': jnp.zeros((D,), jnp.float32)}
    _L0_gnn_all = _L0_gnn_setup()
    _L0_gnn_in = {k: v for k, v in _L0_gnn_all.items() if k in ('w3_w', 'w3_b', 'u3_w', 'u3_b', 'w4_w', 'w4_b', 'w5_w', 'w5_b', 'u5_w', 'u5_b')}
    del _L0_gnn_all
    return {'x': x, 'adj': adj, 'L0_gnn_w3_w': _L0_gnn_in['w3_w'], 'L0_gnn_w3_b': _L0_gnn_in['w3_b'], 'L0_gnn_u3_w': _L0_gnn_in['u3_w'], 'L0_gnn_u3_b': _L0_gnn_in['u3_b'], 'L0_gnn_w4_w': _L0_gnn_in['w4_w'], 'L0_gnn_w4_b': _L0_gnn_in['w4_b'], 'L0_gnn_w5_w': _L0_gnn_in['w5_w'], 'L0_gnn_w5_b': _L0_gnn_in['w5_b'], 'L0_gnn_u5_w': _L0_gnn_in['u5_w'], 'L0_gnn_u5_b': _L0_gnn_in['u5_b']}

def reference(x, adj, L0_gnn_w3_w, L0_gnn_w3_b, L0_gnn_u3_w, L0_gnn_u3_b, L0_gnn_w4_w, L0_gnn_w4_b, L0_gnn_w5_w, L0_gnn_w5_b, L0_gnn_u5_w, L0_gnn_u5_b):
    import jax
    import jax.numpy as jnp

    def _L0_gnn_ref(x, in_mat, out_mat, w3_w, w3_b, u3_w, u3_b, w4_w, w4_b, w5_w, w5_b, u5_w, u5_b):
        import jax, jax.numpy as jnp
        import numpy as np
        B, N, D, T = (64, 128, 256, 3)

        def _lin(v, W, b):
            return jnp.einsum('...i,oi->...o', v, W) + b
        h = x
        for _ in range(T):
            a_in = jnp.einsum('nm,bmd->bnd', in_mat, h)
            a_out = jnp.einsum('nm,bmd->bnd', out_mat, h)
            av = jnp.concatenate([a_in, a_out], axis=-1)
            z = jax.nn.sigmoid(_lin(av, w3_w, w3_b) + _lin(h, u3_w, u3_b))
            r = jax.nn.sigmoid(_lin(av, w4_w, w4_b) + _lin(h, u3_w, u3_b))
            hv = jnp.tanh(_lin(av, w5_w, w5_b) + _lin(r * h, u5_w, u5_b))
            h = (1.0 - z) * h + z * hv
        return h
    x = _layernorm(x + _L0_gnn_ref(x, adj, adj, L0_gnn_w3_w, L0_gnn_w3_b, L0_gnn_u3_w, L0_gnn_u3_b, L0_gnn_w4_w, L0_gnn_w4_b, L0_gnn_w5_w, L0_gnn_w5_b, L0_gnn_u5_w, L0_gnn_u5_b), axis=-1)
    return x

_drawn_inputs = setup_inputs


def setup_inputs(seed=0):
    import zlib

    import numpy as np

    out = dict(_drawn_inputs(seed))
    spreads = {'L0_gnn_w3_b': (0.0, 0.46),
     'L0_gnn_u3_b': (0.0, 0.406),
     'L0_gnn_w4_b': (0.0, 0.8),
     'L0_gnn_w5_b': (0.0, 0.1),
     'L0_gnn_u5_b': (0.0, 0.1)}
    factors = {'L0_gnn_w3_w': 2.889, 'L0_gnn_w4_w': 7.03}
    for name, (base, spread) in spreads.items():
        noise = np.random.default_rng([zlib.crc32(name.encode()), seed]).standard_normal(out[name].shape)
        drawn = base * np.exp(spread * noise) if base else spread * noise
        out[name] = jnp.asarray(drawn.astype(out[name].dtype))
    for name, factor in factors.items():
        out[name] = (out[name] * factor).astype(out[name].dtype)
    return out
```

```python
from contextlib import ExitStack

import concourse.bass as bass
from concourse import mybir

P = 128
F32 = mybir.dt.float32
F32R = mybir.dt.float32r
ALU = mybir.AluOpType
ACT = mybir.ActivationFunctionType

STEPS = 3
EPS = 1e-5
HALVES = 2


def gated_graph_resnorm(nc, x, x_t, adj_t, u3_t, w4_t, w3_t, w5_t, u5_t, biases, out):
    B, N, D = x.shape
    C = N // P
    K = D // P
    PAIRS = B // 2
    UNITS = 2 * STEPS
    HC = C // 2
    assert N == 512 and K == HALVES and C * D == K * N

    with ExitStack() as ctx:
        def sb(name, shape, dt=F32):
            return ctx.enter_context(nc.sbuf_tensor(name, shape, dt))

        def sem(name):
            return ctx.enter_context(nc.semaphore(name))

        ps_agg = ctx.enter_context(nc.psum_tensor("ps_agg", [P, K, N], F32))
        ps_r = ctx.enter_context(nc.psum_tensor("ps_r", [P, K, N], F32))
        ps_z = ctx.enter_context(nc.psum_tensor("ps_z", [P, K, N], F32))
        ps_v = ctx.enter_context(nc.psum_tensor("ps_v", [P, K, N], F32))
        ps_turn = ps_agg[:, :, :].rearrange("p k (c d) -> p (k c) d", d=D)

        x_all = sb("x_all", [P, B, C, D])
        xt = sb("xt", [P, 2, K, N])
        adj_raw = x_all[:, B - 2:B, :, :].rearrange("p b c d -> p (b c d)").rearrange("p (c n) -> p c n", n=N)
        names = ["u3", "w4", "w3", "w5", "u5"]
        halves = {"u3": 1, "w4": 2, "w3": 2, "w5": 2, "u5": 1}
        w_dram = {"u3": u3_t, "w4": w4_t, "w3": w3_t, "w5": w5_t, "u5": u5_t}
        w_raw = {w: sb(f"{w}_raw", [P, halves[w], K, D]) for w in names}
        bias_raw = sb("bias_raw", [P, 5, K])
        bias = sb("bias", [P, 3, K])
        identity = sb("identity", [P, P])

        adj_head, adj_rest = sb("adj_head", [P, C, N], F32R), sb("adj_rest", [P, C, N], F32R)
        w_head = {w: sb(f"{w}_head", [P, K, D], F32R) for w in names}
        w_rest = {w: sb(f"{w}_rest", [P, K, D], F32R) for w in names}
        hn_head, hn_rest = (sb(n, [P, 2, C, D], F32R) for n in ("hn_head", "hn_rest"))
        ht_head, ht_rest = (sb(n, [P, 2, K, N], F32R) for n in ("ht_head", "ht_rest"))
        a_head, a_rest = (sb(n, [P, K, N], F32R) for n in ("a_head", "a_rest"))
        rh_head, rh_rest = (sb(n, [P, K, N], F32R) for n in ("rh_head", "rh_rest"))

        ht = sb("ht", [P, 2, K, N])
        u3h = sb("u3h", [P, K, N])
        r = sb("r", [P, K, N])
        rh = sb("rh", [P, K, N])
        z = sb("z", [P, K, N])
        v = sb("v", [P, K, N])

        stats = sb("stats", [P, 2, C, 6])
        mean_var = sb("mean_var", [P, 2, C, 2])
        var_eps = sb("var_eps", [P, 2, C])
        eps = sb("eps", [P, C])
        minus_half = sb("minus_half", [P, C])
        rstd = sb("rstd", [P, 2, C])

        x_landed = [sem("x_even_landed"), sem("x_odd_landed")]
        xt_landed = [sem("xt_even_landed"), sem("xt_odd_landed")]
        adj_landed = [sem(f"adj{c}_landed") for c in range(C)]
        w_landed = {w: sem(f"{w}_landed") for w in names}
        bias_landed = sem("bias_landed")
        out_stored = sem("out_stored")
        constants_set = sem("constants_set")
        identity_ready = sem("identity_ready")
        bias_ready = sem("bias_ready")
        adj_head_ready = sem("adj_head_ready")
        adj_rest_ready = sem("adj_rest_ready")
        w_summed = sem("w_summed")
        w_head_ready = sem("w_head_ready")
        w_rest_ready = sem("w_rest_ready")
        hn_head_ready = sem("hn_head_ready")
        hn_rest_ready = sem("hn_rest_ready")
        ht_head_ready = sem("ht_head_ready")
        ht_rest_ready = sem("ht_rest_ready")
        agg_done = sem("agg_done")
        u3_done = sem("u3_done")
        r_done = sem("r_done")
        z_done = sem("z_done")
        v_done = sem("v_done")
        turn_done = sem("turn_done")
        a_head_ready = sem("a_head_ready")
        a_rest_ready = sem("a_rest_ready")
        u3_copied = sem("u3_copied")
        r_ready = sem("r_ready")
        rh_ready = sem("rh_ready")
        rh_head_ready = sem("rh_head_ready")
        rh_rest_ready = sem("rh_rest_ready")
        z_summed = sem("z_summed")
        z_ready = sem("z_ready")
        v_ready = sem("v_ready")
        v_minus_h = sem("v_minus_h")
        v_times_z = sem("v_times_z")
        h_ready = sem("h_ready")
        y_ready = sem("y_ready")
        stats_ready = sem("stats_ready")
        moments_ready = sem("moments_ready")
        eps_added = sem("eps_added")
        rstd_ready = sem("rstd_ready")
        out_ready = sem("out_ready")

        x_dram = x.rearrange("b (p c) d -> b p (c d)", c=C)
        out_dram = out.rearrange("b (p c) d -> b p (c d)", c=C)
        xt_dram = x_t.rearrange("b (k p) n -> b p k n", p=P)
        adj_dram = adj_t.rearrange("(p c) n -> p c n", c=C)

        block = ctx.enter_context(nc.Block())

        @block.sync
        def _(sp):
            def load_x(pair, parity):
                sp.dma_start(x_all[:, bass.ds(2 * pair + parity, 1), :, :].rearrange("p b c d -> p b (c d)"),
                             x_dram[bass.ds(2 * pair + parity, 1), :, :].rearrange("b p f -> p b f"),
                             ).then_inc(x_landed[parity], 16)

            def load_xt(pair, parity):
                sp.dma_start(xt[:, parity, :, :],
                             xt_dram[bass.ds(2 * pair + parity, 1), :, :, :].rearrange("b p k n -> p (b k) n"),
                             ).then_inc(xt_landed[parity], 16)

            def store(pair, parity):
                sp.wait_ge(out_ready, 2 * pair + parity + 1)
                sp.dma_start(out_dram[bass.ds(2 * pair + parity, 1), :, :].rearrange("b p f -> p b f"),
                             x_all[:, bass.ds(2 * pair + parity, 1), :, :].rearrange("p b c d -> p b (c d)"),
                             ).then_inc(out_stored, 16)

            def load_next(pair):
                for parity in range(2):
                    sp.wait_ge(x_landed[parity], 16 * (pair + 1))
                    load_x(pair + 1, parity)
                    sp.wait_ge(h_ready, UNITS * pair + parity + 1)
                    load_xt(pair + 1, parity)

            load_x(0, 0)
            for c in range(C):
                sp.dma_start(adj_raw[:, c, :], adj_dram[:, c, :]).then_inc(adj_landed[c], 16)
            load_xt(0, 0)
            for w in names:
                sp.dma_start(w_raw[w][:, :, :, :].rearrange("p a k d -> p (a k d)"), w_dram[w]
                             ).then_inc(w_landed[w], 16)
                if w == "u3":
                    sp.dma_start(bias_raw[:, :, :].rearrange("p b k -> p (b k)"), biases
                                 ).then_inc(bias_landed, 16)
            load_x(0, 1)
            load_xt(0, 1)

            load_next(0)
            with sp.Fori(1, PAIRS - 1) as pair:
                store(pair - 1, 0)
                store(pair - 1, 1)
                load_next(pair)
            for pair in (PAIRS - 2, PAIRS - 1):
                store(pair, 0)
                store(pair, 1)
            sp.wait_ge(out_stored, 16 * B)

        @block.gpsimd
        def _(pool):
            nc.gpsimd.memset(identity[:, :], 0.0).then_inc(constants_set, 1)
            nc.gpsimd.memset(minus_half[:, :], -0.5).then_inc(constants_set, 1)
            nc.gpsimd.memset(eps[:, :], EPS).then_inc(constants_set, 1)
            pool.wait_ge(constants_set, 3)
            nc.gpsimd.affine_select(out=identity[:, :], in_=identity[:, :], compare_op=ALU.not_equal,
                                    fill=1.0, base=0, pattern=[[-1, P]], channel_multiplier=1
                                    ).then_inc(identity_ready, 1)

            def inverse_deviation(graph, parity):
                pool.wait_ge(moments_ready, graph + 1)
                nc.gpsimd.tensor_tensor(var_eps[:, parity, :], mean_var[:, parity, :, 1], eps[:, :], ALU.add
                                        ).then_inc(eps_added, 1)
                pool.wait_ge(eps_added, graph + 1)
                nc.gpsimd.tensor_tensor(rstd[:, parity, :], var_eps[:, parity, :], minus_half[:, :], ALU.pow
                                        ).then_inc(rstd_ready, 1)

            with pool.Fori(0, PAIRS) as pair:
                inverse_deviation(2 * pair, 0)
                inverse_deviation(2 * pair + 1, 1)

        @block.tensor
        def _(pe):
            def product(acc, lhs_head, lhs_rest, rhs_head, rhs_rest, first, last=False, joins=False):
                nc.tensor.matmul(acc, lhs_head, rhs_head, start=first, stop=False, skip_group_check=joins)
                nc.tensor.matmul(acc, lhs_rest, rhs_head, start=False, stop=False, skip_group_check=joins)
                return nc.tensor.matmul(acc, lhs_head, rhs_rest, start=False, stop=last, skip_group_check=joins)

            def weigh(w, acc, head, rest, k, o, first=False, last=False, joins=False):
                cols = slice(o * P, (o + 1) * P)
                return product(acc[:, o, :], w_head[w][:, k, cols], w_rest[w][:, k, cols],
                               head[:, k, :], rest[:, k, :], first, last, joins)

            def turn(parity, u):
                pe.wait_ge(h_ready, u)
                for c in range(C):
                    for k in range(K):
                        last = nc.tensor.transpose(ps_turn[:, c, k * P:(k + 1) * P],
                                                   ht[:, parity, k, c * P:(c + 1) * P], identity[:, :])
                    if c % HC == HC - 1:
                        last.then_inc(turn_done, 1)

            def unit(i, k_unit):
                u = UNITS * i + k_unit
                parity = k_unit % 2
                first_pair = isinstance(i, int) and i == 0
                setup = very_first = first_pair and k_unit == 0

                pe.wait_ge(hn_head_ready, u + 1)
                pe.wait_ge(hn_rest_ready, u + 1)
                if k_unit < 2 and not first_pair:
                    pe.wait_ge(y_ready, 2 * i - 1 + k_unit)
                for k in range(K):
                    for c in range(C):
                        if setup and k == 0:
                            pe.wait_ge(adj_head_ready, c + 1)
                            pe.wait_ge(adj_rest_ready, c + 1)
                        cols = slice(k * P, (k + 1) * P)
                        last = product(ps_agg[:, k, :], hn_head[:, parity, c, cols], hn_rest[:, parity, c, cols],
                                       adj_head[:, c, :], adj_rest[:, c, :], first=c == 0, last=c == C - 1)
                    last.then_inc(agg_done, 1)

                pe.wait_ge(ht_head_ready, u + 1)
                pe.wait_ge(ht_rest_ready, u + 1)
                if setup:
                    pe.wait_ge(w_head_ready, 1)
                    pe.wait_ge(w_rest_ready, 1)
                else:
                    pe.wait_ge(r_ready, 2 * u)
                for o in range(K):
                    for k in range(K):
                        last = weigh("u3", ps_r, ht_head[:, parity], ht_rest[:, parity], k, o,
                                     first=k == 0, last=k == K - 1)
                    last.then_inc(u3_done, 1)

                if setup:
                    pe.wait_ge(w_head_ready, 2)
                    pe.wait_ge(w_rest_ready, 2)
                for o in range(K):
                    pe.wait_ge(u3_copied, 2 * u + o + 1)
                    for k in range(K):
                        if o == 0:
                            pe.wait_ge(a_head_ready, 2 * u + k + 1)
                            pe.wait_ge(a_rest_ready, 2 * u + k + 1)
                        last = weigh("w4", ps_r, a_head, a_rest, k, o, last=k == K - 1, joins=True)
                    last.then_inc(r_done, 1)

                if setup:
                    pe.wait_ge(w_head_ready, 3)
                    pe.wait_ge(w_rest_ready, 3)
                else:
                    pe.wait_ge(z_summed, u)
                for o in range(K):
                    for k in range(K):
                        last = weigh("w3", ps_z, a_head, a_rest, k, o, first=k == 0, last=k == K - 1)
                last.then_inc(z_done, 1)

                if not very_first:
                    turn(1 - parity, u)

                if setup:
                    pe.wait_ge(w_head_ready, 4)
                    pe.wait_ge(w_rest_ready, 4)
                else:
                    pe.wait_ge(v_ready, 2 * u)
                for o in range(K):
                    for k in range(K):
                        weigh("w5", ps_v, a_head, a_rest, k, o, first=k == 0)
                if setup:
                    pe.wait_ge(w_head_ready, 5)
                    pe.wait_ge(w_rest_ready, 5)
                for o in range(K):
                    for k in range(K):
                        if o == 0:
                            pe.wait_ge(rh_head_ready, 2 * u + k + 1)
                            pe.wait_ge(rh_rest_ready, 2 * u + k + 1)
                        last = weigh("u5", ps_v, rh_head, rh_rest, k, o, last=k == K - 1)
                    last.then_inc(v_done, 1)

            pe.wait_ge(identity_ready, 1)
            for k_unit in range(UNITS):
                unit(0, k_unit)
            with pe.Fori(1, PAIRS) as i:
                for k_unit in range(UNITS):
                    unit(i, k_unit)
            turn(1, UNITS * PAIRS)

        @block.scalar
        def _(act):
            def candidate(u):
                for o in range(K):
                    act.wait_ge(v_done, 2 * u - 1 + o)
                    nc.scalar.activation(v[:, o, :], ps_v[:, o, :], ACT.Tanh, bias=bias[:, 2, o:o + 1]
                                         ).then_inc(v_ready, 1)

            def aggregation_head(u, k):
                act.wait_ge(agg_done, 2 * u + k + 1)
                nc.scalar.copy(a_head[:, k, :], ps_agg[:, k, :]).then_inc(a_head_ready, 1)

            def split_x_t(pair, parity):
                act.wait_ge(xt_landed[parity], 16 * (pair + 1))
                nc.scalar.copy(ht_head[:, parity, :, :], xt[:, parity, :, :]).then_inc(ht_head_ready, 1)

            def split_x(pair, parity):
                act.wait_ge(x_landed[parity], 16 * (pair + 1))
                nc.scalar.copy(hn_head[:, parity, :, :].rearrange("p c d -> p (c d)"),
                               x_all[:, bass.ds(2 * pair + parity, 1), :, :].rearrange("p b c d -> p (b c d)"),
                               ).then_inc(hn_head_ready, 1)

            def unit(i, k_unit, last_pair=False):
                u = UNITS * i + k_unit
                other = 1 - k_unit % 2
                very_first = isinstance(i, int) and i == 0 and k_unit == 0
                ended = k_unit in (0, UNITS - 1)
                following = not (last_pair and k_unit == UNITS - 1)
                pair = i if k_unit == 0 else i + 1

                if not very_first:
                    candidate(u)
                aggregation_head(u, 0)
                if not ended:
                    act.wait_ge(h_ready, u)
                    nc.scalar.copy(ht_head[:, other, :, :], ht[:, other, :, :]).then_inc(ht_head_ready, 1)
                elif following:
                    split_x_t(pair, other)
                aggregation_head(u, 1)
                for o in range(K):
                    act.wait_ge(u3_done, 2 * u + o + 1)
                    nc.scalar.copy(u3h[:, o, :], ps_r[:, o, :]).then_inc(u3_copied, 1)
                for o in range(K):
                    act.wait_ge(r_done, 2 * u + o + 1)
                    nc.scalar.activation(r[:, o, :], ps_r[:, o, :], ACT.Sigmoid, bias=bias[:, 1, o:o + 1]
                                         ).then_inc(r_ready, 1)
                for k in range(K):
                    act.wait_ge(rh_ready, 2 * u + k + 1)
                    nc.scalar.copy(rh_head[:, k, :], rh[:, k, :]).then_inc(rh_head_ready, 1)
                if not ended:
                    act.wait_ge(turn_done, 2 * u)
                    nc.scalar.copy(hn_head[:, other, :, :], ps_turn).then_inc(hn_head_ready, 1)
                elif following:
                    split_x(pair, other)
                act.wait_ge(z_summed, u + 1)
                for o in range(K):
                    nc.scalar.activation(z[:, o, :], z[:, o, :], ACT.Sigmoid, bias=bias[:, 0, o:o + 1]
                                         ).then_inc(z_ready, 1)

            split_x(0, 0)
            for c in range(C):
                act.wait_ge(adj_landed[c], 16)
                nc.scalar.copy(adj_head[:, c, :], adj_raw[:, c, :]).then_inc(adj_head_ready, 1)
            split_x_t(0, 0)
            for n, w in enumerate(names):
                if halves[w] == 2:
                    act.wait_ge(w_summed, n)
                else:
                    act.wait_ge(w_landed[w], 16)
                nc.scalar.copy(w_head[w][:, :, :], w_raw[w][:, 0, :, :]).then_inc(w_head_ready, 1)
            act.wait_ge(bias_ready, 3)

            for k_unit in range(UNITS):
                unit(0, k_unit)
            with act.Fori(1, PAIRS - 1) as i:
                for k_unit in range(UNITS):
                    unit(i, k_unit)
            for k_unit in range(UNITS):
                unit(PAIRS - 1, k_unit, last_pair=True)
            candidate(UNITS * PAIRS)

        @block.vector
        def _(dve):
            def rest(out_, whole, head):
                return nc.vector.tensor_tensor(out_, whole, head.bitcast(F32), ALU.subtract)

            def aggregation_rest(u, k):
                dve.wait_ge(a_head_ready, 2 * u + k + 1)
                rest(a_rest[:, k, :], ps_agg[:, k, :], a_head[:, k, :]).then_inc(a_rest_ready, 1)

            def split_x_t(pair, parity):
                dve.wait_ge(ht_head_ready, UNITS * pair + parity + 1)
                rest(ht_rest[:, parity, :, :], xt[:, parity, :, :], ht_head[:, parity, :, :]
                     ).then_inc(ht_rest_ready, 1)

            def split_x(pair, parity):
                dve.wait_ge(hn_head_ready, UNITS * pair + parity + 1)
                rest(hn_rest[:, parity, :, :].rearrange("p c d -> p (c d)"),
                     x_all[:, bass.ds(2 * pair + parity, 1), :, :].rearrange("p b c d -> p (b c d)"),
                     hn_head[:, parity, :, :].rearrange("p c d -> p (c d)")).then_inc(hn_rest_ready, 1)

            def candidate_less_state(u, h):
                dve.wait_ge(v_ready, 2 * u)
                nc.vector.tensor_tensor(v[:, :, :], v[:, :, :], h, ALU.subtract).then_inc(v_minus_h, 1)
                dve.wait_ge(v_minus_h, u)
                dve.wait_ge(z_ready, 2 * u)
                nc.vector.tensor_tensor(v[:, :, :], v[:, :, :], z[:, :, :], ALU.mult).then_inc(v_times_z, 1)

            def new_state(u, parity, h):
                dve.wait_ge(v_times_z, u)
                nc.vector.tensor_tensor(ht[:, parity, :, :], v[:, :, :], h, ALU.add).then_inc(h_ready, 1)

            def rows(pair, parity):
                graph = x_all[:, bass.ds(2 * pair + parity, 1), :, :]
                return graph.rearrange("p b c d -> p (b c) d")

            def residual(u, pair, parity):
                y = rows(pair, parity)
                dve.wait_ge(turn_done, 2 * u)
                nc.vector.tensor_tensor(y, ps_turn, y, ALU.add).then_inc(y_ready, 1)

            def statistics(pair, parity):
                y = rows(pair, parity)
                for c in range(C):
                    last = nc.vector.bn_stats(stats[:, parity, c, :], y[:, c, :])
                last.then_inc(stats_ready, 1)

            def moments(parity):
                for c in range(C):
                    last = nc.vector.bn_aggr(mean_var[:, parity, c, :], stats[:, parity, c, :])
                last.then_inc(moments_ready, 1)

            def normalise(pair, parity):
                y = rows(pair, parity)
                dve.wait_ge(rstd_ready, 2 * pair + parity + 1)
                for c in range(C):
                    last = nc.vector.tensor_scalar(y[:, c, :], y[:, c, :], mean_var[:, parity, c, 0:1],
                                                   rstd[:, parity, c:c + 1], ALU.subtract, ALU.mult)
                last.then_inc(out_ready, 1)

            def state(k_unit):
                return xt[:, k_unit % 2, :, :] if k_unit < 2 else ht[:, k_unit % 2, :, :]

            def unit(i, k_unit, last_pair=False):
                u = UNITS * i + k_unit
                parity, other = k_unit % 2, 1 - k_unit % 2
                first_pair = isinstance(i, int) and i == 0
                very_first = first_pair and k_unit == 0
                ended = k_unit in (0, UNITS - 1)
                following = not (last_pair and k_unit == UNITS - 1)
                pair = i if k_unit == 0 else i + 1
                h_before = state((k_unit - 1) % UNITS)

                if not very_first:
                    candidate_less_state(u, h_before)
                if k_unit < 2 and not first_pair:
                    dve.wait_ge(stats_ready, 2 * i - 1 + k_unit)
                aggregation_rest(u, 0)
                if not very_first:
                    new_state(u, other, h_before)
                if k_unit < 2 and not first_pair:
                    moments(parity)
                aggregation_rest(u, 1)
                if not ended:
                    dve.wait_ge(ht_head_ready, u + 2)
                    rest(ht_rest[:, other, :, :], ht[:, other, :, :], ht_head[:, other, :, :]
                         ).then_inc(ht_rest_ready, 1)
                elif following:
                    split_x_t(pair, other)
                if k_unit < 2 and not first_pair:
                    normalise(i - 1, parity)
                h = state(k_unit)
                for k in range(K):
                    dve.wait_ge(r_ready, 2 * u + k + 1)
                    nc.vector.tensor_tensor(rh[:, k, :], r[:, k, :], h[:, k, :], ALU.mult).then_inc(rh_ready, 1)
                for k in range(K):
                    dve.wait_ge(rh_head_ready, 2 * u + k + 1)
                    rest(rh_rest[:, k, :], rh[:, k, :], rh_head[:, k, :]).then_inc(rh_rest_ready, 1)
                dve.wait_ge(z_done, u + 1)
                dve.wait_ge(u3_copied, 2 * u + 2)
                nc.vector.tensor_tensor(z[:, :, :], ps_z[:, :, :], u3h[:, :, :], ALU.add).then_inc(z_summed, 1)
                if not ended:
                    dve.wait_ge(hn_head_ready, u + 2)
                    rest(hn_rest[:, other, :, :], ps_turn, hn_head[:, other, :, :]
                         ).then_inc(hn_rest_ready, 1)
                else:
                    if not very_first:
                        residual(u, i if k_unit else i - 1, other)
                        dve.wait_ge(y_ready, 2 * i + (1 if k_unit else 0))
                    if following:
                        split_x(pair, other)
                    if not very_first:
                        statistics(i if k_unit else i - 1, other)

            split_x(0, 0)
            for c in range(C):
                dve.wait_ge(adj_head_ready, c + 1)
                rest(adj_rest[:, c, :], adj_raw[:, c, :], adj_head[:, c, :]).then_inc(adj_rest_ready, 1)
            split_x_t(0, 0)
            dve.wait_ge(bias_landed, 16)
            for n, (b, c) in enumerate(((0, 1), (2, 1), (3, 4))):
                nc.vector.tensor_tensor(bias[:, n, :], bias_raw[:, b, :], bias_raw[:, c, :], ALU.add
                                        ).then_inc(bias_ready, 1)
            for n, w in enumerate(names):
                if halves[w] == 2:
                    dve.wait_ge(w_landed[w], 16)
                    nc.vector.tensor_tensor(w_raw[w][:, 0, :, :], w_raw[w][:, 0, :, :], w_raw[w][:, 1, :, :],
                                            ALU.add).then_inc(w_summed, 1)
                dve.wait_ge(w_head_ready, n + 1)
                rest(w_rest[w][:, :, :], w_raw[w][:, 0, :, :], w_head[w][:, :, :]).then_inc(w_rest_ready, 1)

            for k_unit in range(UNITS):
                unit(0, k_unit)
            with dve.Fori(1, PAIRS - 1) as i:
                for k_unit in range(UNITS):
                    unit(i, k_unit)
            for k_unit in range(UNITS):
                unit(PAIRS - 1, k_unit, last_pair=True)
            units = UNITS * PAIRS
            dve.wait_ge(stats_ready, B - 1)
            moments(0)
            candidate_less_state(units, state(UNITS - 1))
            new_state(units, 1, state(UNITS - 1))
            normalise(PAIRS - 1, 0)
            residual(units, PAIRS - 1, 1)
            dve.wait_ge(y_ready, B)
            statistics(PAIRS - 1, 1)
            dve.wait_ge(stats_ready, B)
            moments(1)
            normalise(PAIRS - 1, 1)


def kernel(x, adj, L0_gnn_w3_w, L0_gnn_w3_b, L0_gnn_u3_w, L0_gnn_u3_b, L0_gnn_w4_w, L0_gnn_w4_b,
           L0_gnn_w5_w, L0_gnn_w5_b, L0_gnn_u5_w, L0_gnn_u5_b):
    import numpy as np
    import concourse.bacc as bacc
    from concourse.bass_utils import run_bass_kernel_spmd

    B, N, D = x.shape
    C = N // P
    x, adj = np.asarray(x), np.asarray(adj)

    def weights(w):
        w = np.asarray(w)
        return np.ascontiguousarray(w.T.reshape(-1, P, D).transpose(1, 0, 2).reshape(P, -1))

    arrays = {
        "x": np.ascontiguousarray(x),
        "x_t": np.ascontiguousarray(x.reshape(B, P, C, D).transpose(0, 3, 2, 1).reshape(B, D, N)),
        "adj_t": np.ascontiguousarray(adj.reshape(P, C, N).transpose(2, 1, 0).reshape(N, N)),
        "u3_t": weights(L0_gnn_u3_w),
        "w4_t": weights(L0_gnn_w4_w),
        "w3_t": weights(L0_gnn_w3_w),
        "w5_t": weights(L0_gnn_w5_w),
        "u5_t": weights(L0_gnn_u5_w),
        "biases": np.ascontiguousarray(
            np.stack([np.asarray(b) for b in (L0_gnn_w3_b, L0_gnn_u3_b, L0_gnn_w4_b, L0_gnn_w5_b, L0_gnn_u5_b)])
            .reshape(5, D // P, P).transpose(2, 0, 1).reshape(P, -1)),
    }
    nc = bacc.Bacc("TRN2", target_bir_lowering=False, num_devices=1)
    args = [nc.dram_tensor(f"in_{n}", a.shape, F32, kind="ExternalInput").ap() for n, a in arrays.items()]
    args.append(nc.dram_tensor("out", (B, N, D), F32, kind="ExternalOutput").ap())
    gated_graph_resnorm(nc, *args)
    result = run_bass_kernel_spmd(nc, [{f"in_{n}": a for n, a in arrays.items()}], core_ids=[0])
    return result.results[0]["out"]
```

```python
from contextlib import ExitStack

import concourse.bass as bass
from concourse import mybir

P = 128
F32 = mybir.dt.float32
F32R = mybir.dt.float32r
ALU = mybir.AluOpType
ACT = mybir.ActivationFunctionType

STEPS = 3
EPS = 1e-5
HALVES = 2


def gated_graph_resnorm(nc, B, N, D, x, x_t, adj_t, u3_t, w4_t, w3_t, w5_t, u5_t, biases, out):
    C = N // P
    K = D // P
    PAIRS = B // 2
    UNITS = 2 * STEPS
    Q = P // 32
    E = 32
    QF = C * D // Q
    assert N == 512 and K == HALVES and C * D == K * N

    with ExitStack() as ctx:
        def sb(name, shape, dt=F32):
            return ctx.enter_context(nc.sbuf_tensor(name, shape, dt))

        def sem(name):
            return ctx.enter_context(nc.semaphore(name))

        ps_agg = ctx.enter_context(nc.psum_tensor("ps_agg", [P, K, N], F32))
        ps_r = ctx.enter_context(nc.psum_tensor("ps_r", [P, K, N], F32))
        ps_z = ctx.enter_context(nc.psum_tensor("ps_z", [P, K, N], F32))
        ps_v = ctx.enter_context(nc.psum_tensor("ps_v", [P, K, N], F32))

        x_all = sb("x_all", [P, B, C * D])
        xt = sb("xt", [P, 2, K, N])
        adj_raw = x_all[:, B - 2:B, :].rearrange("p b f -> p (b f)").rearrange("p (c n) -> p c n", n=N)
        names = ["u3", "w4", "w3", "w5", "u5"]
        halves = {"u3": 1, "w4": 2, "w3": 2, "w5": 2, "u5": 1}
        w_dram = {"u3": u3_t, "w4": w4_t, "w3": w3_t, "w5": w5_t, "u5": u5_t}
        w_raw = {w: x_all[:, B - 3 - n, 0:halves[w] * K * D].rearrange("p (a k d) -> p a k d", k=K, d=D)
                 for n, w in enumerate(names)}
        bias_raw = sb("bias_raw", [P, 5, K])
        bias = sb("bias", [P, 3, K])

        adj_head, adj_rest = sb("adj_head", [P, C, N], F32R), sb("adj_rest", [P, C, N], F32R)
        w_head = {w: sb(f"{w}_head", [P, K, D], F32R) for w in names}
        w_rest = {w: sb(f"{w}_rest", [P, K, D], F32R) for w in names}
        hn_head, hn_rest = (sb(n, [P, 2, C, D], F32R) for n in ("hn_head", "hn_rest"))
        ht_head, ht_rest = (sb(n, [P, 2, K, N], F32R) for n in ("ht_head", "ht_rest"))
        a_head, a_rest = (sb(n, [P, K, N], F32R) for n in ("a_head", "a_rest"))
        rh_head, rh_rest = (sb(n, [P, K, N], F32R) for n in ("rh_head", "rh_rest"))

        ht = sb("ht", [P, 2, K, N])
        h_blocks = sb("h_blocks", [P, Q, K * C * E])
        hn = sb("hn", [P, Q, QF])
        u3h = sb("u3h", [P, K, N])
        r = sb("r", [P, K, N])
        rh = sb("rh", [P, K, N])
        z = sb("z", [P, K, N])
        v = sb("v", [P, K, N])

        stats = sb("stats", [P, 2, C, 6])
        mean_var = sb("mean_var", [P, 2, C, 2])
        var_eps = sb("var_eps", [P, 2, C])
        eps = sb("eps", [P, C])
        minus_half = sb("minus_half", [P, C])
        rstd = sb("rstd", [P, 2, C])

        x_landed = [sem("x_even_landed"), sem("x_odd_landed")]
        xt_landed = [sem("xt_even_landed"), sem("xt_odd_landed")]
        adj_landed = [sem(f"adj{c}_landed") for c in range(C)]
        w_landed = {w: sem(f"{w}_landed") for w in names}
        bias_landed = sem("bias_landed")
        out_stored = sem("out_stored")
        constants_set = sem("constants_set")
        bias_ready = sem("bias_ready")
        adj_head_ready = sem("adj_head_ready")
        adj_rest_ready = sem("adj_rest_ready")
        w_summed = sem("w_summed")
        w_head_ready = sem("w_head_ready")
        w_rest_ready = sem("w_rest_ready")
        hn_head_ready = sem("hn_head_ready")
        hn_rest_ready = sem("hn_rest_ready")
        ht_head_ready = sem("ht_head_ready")
        ht_rest_ready = sem("ht_rest_ready")
        agg_done = sem("agg_done")
        u3_done = sem("u3_done")
        r_done = sem("r_done")
        z_done = sem("z_done")
        v_done = sem("v_done")
        a_head_ready = sem("a_head_ready")
        a_rest_ready = sem("a_rest_ready")
        u3_copied = sem("u3_copied")
        r_ready = sem("r_ready")
        rh_ready = sem("rh_ready")
        rh_head_ready = sem("rh_head_ready")
        rh_rest_ready = sem("rh_rest_ready")
        z_summed = sem("z_summed")
        z_ready = sem("z_ready")
        v_ready = sem("v_ready")
        v_minus_h = sem("v_minus_h")
        v_times_z = sem("v_times_z")
        h_ready = sem("h_ready")
        blocks_ready = sem("blocks_ready")
        hn_moved = sem("hn_moved")
        y_ready = sem("y_ready")
        stats_ready = sem("stats_ready")
        moments_ready = sem("moments_ready")
        eps_added = sem("eps_added")
        rstd_ready = sem("rstd_ready")
        out_ready = sem("out_ready")

        xt_dram = x_t.rearrange("b (k p) n -> b p k n", p=P)
        adj_dram = adj_t.rearrange("(p c) n -> p c n", c=C)

        block = ctx.enter_context(nc.Block())

        @block.sync
        def _(sp):
            def load_x(pair, parity):
                sp.dma_start(x_all[:, bass.ds(2 * pair + parity, 1), :],
                             x[bass.ds(2 * pair + parity, 1), :, :].rearrange("b p f -> p b f"),
                             ).then_inc(x_landed[parity], 16)

            def load_xt(pair, parity):
                sp.dma_start(xt[:, parity, :, :],
                             xt_dram[bass.ds(2 * pair + parity, 1), :, :, :].rearrange("b p k n -> p (b k) n"),
                             ).then_inc(xt_landed[parity], 16)

            def store(pair, parity):
                sp.wait_ge(out_ready, 2 * pair + parity + 1)
                sp.dma_start(out[bass.ds(2 * pair + parity, 1), :, :].rearrange("b p f -> p b f"),
                             x_all[:, bass.ds(2 * pair + parity, 1), :],
                             ).then_inc(out_stored, 16)

            def load_next(pair):
                for parity in range(2):
                    sp.wait_ge(x_landed[parity], 16 * (pair + 1))
                    load_x(pair + 1, parity)
                    sp.wait_ge(h_ready, 2 * (UNITS * pair + parity + 1))
                    load_xt(pair + 1, parity)

            load_x(0, 0)
            for c in range(C):
                sp.dma_start(adj_raw[:, c, :], adj_dram[:, c, :]).then_inc(adj_landed[c], 16)
            load_xt(0, 0)
            for w in names:
                sp.dma_start(w_raw[w].rearrange("p a k d -> p (a k d)"), w_dram[w]
                             ).then_inc(w_landed[w], 16)
                if w == "u3":
                    sp.dma_start(bias_raw[:, :, :].rearrange("p b k -> p (b k)"), biases
                                 ).then_inc(bias_landed, 16)
            load_x(0, 1)
            load_xt(0, 1)

            load_next(0)
            with sp.Fori(1, PAIRS - 1) as pair:
                store(pair - 1, 0)
                store(pair - 1, 1)
                load_next(pair)
            for pair in (PAIRS - 2, PAIRS - 1):
                store(pair, 0)
                store(pair, 1)
            sp.wait_ge(out_stored, 16 * B)

        @block.gpsimd
        def _(pool):
            nc.gpsimd.memset(minus_half[:, :], -0.5).then_inc(constants_set, 1)
            nc.gpsimd.memset(eps[:, :], EPS).then_inc(constants_set, 1)
            pool.wait_ge(constants_set, 2)

            def inverse_deviation(graph, parity):
                pool.wait_ge(moments_ready, graph + 1)
                nc.gpsimd.tensor_tensor(var_eps[:, parity, :], mean_var[:, parity, :, 1], eps[:, :], ALU.add
                                        ).then_inc(eps_added, 1)
                pool.wait_ge(eps_added, graph + 1)
                nc.gpsimd.tensor_tensor(rstd[:, parity, :], var_eps[:, parity, :], minus_half[:, :], ALU.pow
                                        ).then_inc(rstd_ready, 1)

            with pool.Fori(0, PAIRS) as pair:
                inverse_deviation(2 * pair, 0)
                inverse_deviation(2 * pair + 1, 1)

        @block.tensor
        def _(pe):
            def product(acc, lhs_head, lhs_rest, rhs_head, rhs_rest, first, last=False, joins=False):
                nc.tensor.matmul(acc, lhs_head, rhs_head, start=first, stop=False, skip_group_check=joins)
                nc.tensor.matmul(acc, lhs_rest, rhs_head, start=False, stop=False, skip_group_check=joins)
                return nc.tensor.matmul(acc, lhs_head, rhs_rest, start=False, stop=last, skip_group_check=joins)

            def weigh(w, acc, head, rest, k, o, first=False, last=False, joins=False):
                cols = slice(o * P, (o + 1) * P)
                return product(acc[:, o, :], w_head[w][:, k, cols], w_rest[w][:, k, cols],
                               head[:, k, :], rest[:, k, :], first, last, joins)

            def unit(i, k_unit):
                u = UNITS * i + k_unit
                parity = k_unit % 2
                first_pair = isinstance(i, int) and i == 0
                setup = very_first = first_pair and k_unit == 0

                pe.wait_ge(hn_head_ready, u + 1)
                for k in range(K):
                    for c in range(C):
                        if setup and k == 0:
                            pe.wait_ge(adj_head_ready, c + 1)
                            pe.wait_ge(adj_rest_ready, c + 1)
                        nc.tensor.matmul(ps_agg[:, k, :], hn_head[:, parity, c, k * P:(k + 1) * P], adj_head[:, c, :],
                                         start=c == 0, stop=False)
                        nc.tensor.matmul(ps_agg[:, k, :], hn_head[:, parity, c, k * P:(k + 1) * P], adj_rest[:, c, :],
                                         start=False, stop=False)
                    if k == 0:
                        pe.wait_ge(hn_rest_ready, u + 1)
                    for c in range(C):
                        last = nc.tensor.matmul(ps_agg[:, k, :], hn_rest[:, parity, c, k * P:(k + 1) * P], adj_head[:, c, :],
                                                start=False, stop=c == C - 1)
                    last.then_inc(agg_done, 1)

                pe.wait_ge(ht_head_ready, u + 1)
                pe.wait_ge(ht_rest_ready, u + 1)
                if setup:
                    pe.wait_ge(w_head_ready, 1)
                    pe.wait_ge(w_rest_ready, 1)
                else:
                    pe.wait_ge(r_ready, 2 * u)
                for o in range(K):
                    for k in range(K):
                        last = weigh("u3", ps_r, ht_head[:, parity], ht_rest[:, parity], k, o,
                                     first=k == 0, last=k == K - 1)
                    last.then_inc(u3_done, 1)

                if setup:
                    pe.wait_ge(w_head_ready, 2)
                    pe.wait_ge(w_rest_ready, 2)
                for o in range(K):
                    pe.wait_ge(u3_copied, 2 * u + o + 1)
                    for k in range(K):
                        if o == 0:
                            pe.wait_ge(a_head_ready, 2 * u + k + 1)
                            pe.wait_ge(a_rest_ready, 2 * u + k + 1)
                        last = weigh("w4", ps_r, a_head, a_rest, k, o, last=k == K - 1, joins=True)
                    last.then_inc(r_done, 1)

                if setup:
                    pe.wait_ge(w_head_ready, 3)
                    pe.wait_ge(w_rest_ready, 3)
                else:
                    pe.wait_ge(z_summed, u)
                for o in range(K):
                    for k in range(K):
                        last = weigh("w3", ps_z, a_head, a_rest, k, o, first=k == 0, last=k == K - 1)
                last.then_inc(z_done, 1)

                if setup:
                    pe.wait_ge(w_head_ready, 4)
                    pe.wait_ge(w_rest_ready, 4)
                else:
                    pe.wait_ge(v_ready, 2 * u)
                for o in range(K):
                    for k in range(K):
                        weigh("w5", ps_v, a_head, a_rest, k, o, first=k == 0)
                if setup:
                    pe.wait_ge(w_head_ready, 5)
                    pe.wait_ge(w_rest_ready, 5)
                for o in range(K):
                    for k in range(K):
                        if o == 0:
                            pe.wait_ge(rh_head_ready, 2 * u + k + 1)
                            pe.wait_ge(rh_rest_ready, 2 * u + k + 1)
                        last = weigh("u5", ps_v, rh_head, rh_rest, k, o, last=k == K - 1)
                    last.then_inc(v_done, 1)

            for k_unit in range(UNITS):
                unit(0, k_unit)
            with pe.Fori(1, PAIRS) as i:
                for k_unit in range(UNITS):
                    unit(i, k_unit)

        @block.scalar
        def _(act):
            def candidate(u):
                for o in range(K):
                    act.wait_ge(v_done, 2 * u - 1 + o)
                    nc.scalar.activation(v[:, o, :], ps_v[:, o, :], ACT.Tanh, bias=bias[:, 2, o:o + 1]
                                         ).then_inc(v_ready, 1)

            def aggregation_head(u, k):
                act.wait_ge(agg_done, 2 * u + k + 1)
                nc.scalar.copy(a_head[:, k, :], ps_agg[:, k, :]).then_inc(a_head_ready, 1)

            def split_x_t(pair, parity):
                act.wait_ge(xt_landed[parity], 16 * (pair + 1))
                nc.scalar.copy(ht_head[:, parity, :, :], xt[:, parity, :, :]).then_inc(ht_head_ready, 1)

            def move(n, count):
                for m in range(n, n + count):
                    q, j = m // Q, m % Q
                    last = nc.scalar.copy(hn[E * j:E * (j + 1), q, :], h_blocks[E * q:E * (q + 1), j, :])
                if n + count == Q * Q:
                    last.then_inc(hn_moved, 1)

            def unit(i, k_unit, last_pair=False):
                u = UNITS * i + k_unit
                other = 1 - k_unit % 2
                very_first = isinstance(i, int) and i == 0 and k_unit == 0
                ended = k_unit in (0, UNITS - 1)
                following = not (last_pair and k_unit == UNITS - 1)
                pair = i if k_unit == 0 else i + 1

                if not very_first:
                    candidate(u)
                aggregation_head(u, 0)
                if not ended:
                    act.wait_ge(h_ready, 2 * u)
                    nc.scalar.copy(ht_head[:, other, :, :], ht[:, other, :, :]).then_inc(ht_head_ready, 1)
                elif following:
                    split_x_t(pair, other)
                aggregation_head(u, 1)
                if not very_first:
                    act.wait_ge(blocks_ready, u)
                    move(0, 2)
                for o in range(K):
                    act.wait_ge(u3_done, 2 * u + o + 1)
                    nc.scalar.copy(u3h[:, o, :], ps_r[:, o, :]).then_inc(u3_copied, 1)
                    if not very_first:
                        move(2 + 3 * o, 3)
                for o in range(K):
                    act.wait_ge(r_done, 2 * u + o + 1)
                    nc.scalar.activation(r[:, o, :], ps_r[:, o, :], ACT.Sigmoid, bias=bias[:, 1, o:o + 1]
                                         ).then_inc(r_ready, 1)
                    if not very_first and o == 0:
                        move(8, 2)
                for k in range(K):
                    act.wait_ge(rh_ready, 2 * u + k + 1)
                    nc.scalar.copy(rh_head[:, k, :], rh[:, k, :]).then_inc(rh_head_ready, 1)
                if not very_first:
                    move(10, 6)
                act.wait_ge(z_summed, u + 1)
                for o in range(K):
                    nc.scalar.activation(z[:, o, :], z[:, o, :], ACT.Sigmoid, bias=bias[:, 0, o:o + 1]
                                         ).then_inc(z_ready, 1)

            for c in range(C):
                act.wait_ge(adj_landed[c], 16)
                nc.scalar.copy(adj_head[:, c, :], adj_raw[:, c, :]).then_inc(adj_head_ready, 1)
            split_x_t(0, 0)
            for n, w in enumerate(names):
                if halves[w] == 2:
                    act.wait_ge(w_summed, n)
                else:
                    act.wait_ge(w_landed[w], 16)
                nc.scalar.copy(w_head[w][:, :, :], w_raw[w][:, 0, :, :]).then_inc(w_head_ready, 1)
            act.wait_ge(bias_ready, 3)

            for k_unit in range(UNITS):
                unit(0, k_unit)
            with act.Fori(1, PAIRS - 1) as i:
                for k_unit in range(UNITS):
                    unit(i, k_unit)
            for k_unit in range(UNITS):
                unit(PAIRS - 1, k_unit, last_pair=True)
            candidate(UNITS * PAIRS)
            act.wait_ge(blocks_ready, UNITS * PAIRS)
            move(0, Q * Q)

        @block.vector
        def _(dve):
            def rest(out_, whole, head):
                return nc.vector.tensor_tensor(out_, whole, head.bitcast(F32), ALU.subtract)

            def aggregation_rest(u, k):
                dve.wait_ge(a_head_ready, 2 * u + k + 1)
                rest(a_rest[:, k, :], ps_agg[:, k, :], a_head[:, k, :]).then_inc(a_rest_ready, 1)

            def split_x_t(pair, parity):
                dve.wait_ge(ht_head_ready, UNITS * pair + parity + 1)
                rest(ht_rest[:, parity, :, :], xt[:, parity, :, :], ht_head[:, parity, :, :]
                     ).then_inc(ht_rest_ready, 1)

            def by_chunk(t, parity):
                return t[:, parity, :, :].rearrange("p c (f e) -> p f c e", e=E)

            def split_nodes(whole, parity, n):
                whole = whole.rearrange("p (f c e) -> p f c e", c=C, e=E)
                nc.vector.tensor_scalar(by_chunk(hn_head, parity), whole, 1.0, None, ALU.mult
                                        ).then_inc(hn_head_ready, 1)
                dve.wait_ge(hn_head_ready, n)
                rest(by_chunk(hn_rest, parity), whole, by_chunk(hn_head, parity)).then_inc(hn_rest_ready, 1)

            def split_x(pair, parity):
                dve.wait_ge(x_landed[parity], 16 * (pair + 1))
                split_nodes(rows(pair, parity), parity, UNITS * pair + parity + 1)

            def split_hn(u, parity):
                dve.wait_ge(hn_moved, u)
                split_nodes(hn[:, :, :].rearrange("p q f -> p (q f)"), parity, u + 2)

            def less_state(u, o, h):
                dve.wait_ge(v_ready, 2 * u - 1 + o)
                nc.vector.tensor_tensor(v[:, o, :], v[:, o, :], h[:, o, :], ALU.subtract).then_inc(v_minus_h, 1)

            def times_z(u, o):
                dve.wait_ge(v_minus_h, 2 * u - 1 + o)
                dve.wait_ge(z_ready, 2 * u - 1 + o)
                nc.vector.tensor_tensor(v[:, o, :], v[:, o, :], z[:, o, :], ALU.mult).then_inc(v_times_z, 1)

            def plus_state(u, o, h, parity):
                dve.wait_ge(v_times_z, 2 * u - 1 + o)
                nc.vector.tensor_tensor(ht[:, parity, o, :], v[:, o, :], h[:, o, :], ALU.add).then_inc(h_ready, 1)

            def new_state(u, h, parity):
                less_state(u, 0, h)
                times_z(u, 0)
                less_state(u, 1, h)
                plus_state(u, 0, h, parity)
                times_z(u, 1)
                plus_state(u, 1, h, parity)

            def transpose_blocks(u, parity):
                dve.wait_ge(h_ready, 2 * u)
                nc.vector.transpose(h_blocks[:, :, :].rearrange("p j (f e) -> p j f e", e=E),
                                    ht[:, parity, :, :].rearrange("p k n -> p (k n)")
                                    .rearrange("p (f j i) -> p j f i", j=Q, i=E)).then_inc(blocks_ready, 1)

            def rows(pair, parity):
                return x_all[:, bass.ds(2 * pair + parity, 1), :].rearrange("p b f -> p (b f)")

            def chunk(y, c):
                return y.rearrange("p (f c e) -> p f c e", c=C, e=E)[:, :, c, :]

            def residual(u, pair, parity):
                y = rows(pair, parity)
                dve.wait_ge(hn_moved, u)
                nc.vector.tensor_tensor(y, hn[:, :, :].rearrange("p q f -> p (q f)"), y, ALU.add).then_inc(y_ready, 1)

            def statistics(pair, parity):
                y = rows(pair, parity)
                for c in range(C):
                    last = nc.vector.bn_stats(stats[:, parity, c, :], chunk(y, c))
                last.then_inc(stats_ready, 1)

            def moments(parity):
                for c in range(C):
                    last = nc.vector.bn_aggr(mean_var[:, parity, c, :], stats[:, parity, c, :])
                last.then_inc(moments_ready, 1)

            def normalise(pair, parity):
                y = rows(pair, parity)
                dve.wait_ge(rstd_ready, 2 * pair + parity + 1)
                for c in range(C):
                    last = nc.vector.tensor_scalar(chunk(y, c), chunk(y, c), mean_var[:, parity, c, 0:1],
                                                   rstd[:, parity, c:c + 1], ALU.subtract, ALU.mult)
                last.then_inc(out_ready, 1)

            def state(k_unit):
                return xt[:, k_unit % 2, :, :] if k_unit < 2 else ht[:, k_unit % 2, :, :]

            def unit(i, k_unit, last_pair=False):
                u = UNITS * i + k_unit
                parity, other = k_unit % 2, 1 - k_unit % 2
                first_pair = isinstance(i, int) and i == 0
                very_first = first_pair and k_unit == 0
                ended = k_unit in (0, UNITS - 1)
                following = not (last_pair and k_unit == UNITS - 1)
                pair = i if k_unit == 0 else i + 1
                h_before = state((k_unit - 1) % UNITS)
                normed = k_unit < 2 and not first_pair

                if not very_first:
                    new_state(u, h_before, other)
                if normed:
                    dve.wait_ge(y_ready, 2 * i - 1 + k_unit)
                aggregation_rest(u, 0)
                if normed:
                    statistics(i - 1, parity)
                if not very_first:
                    transpose_blocks(u, other)
                if normed:
                    dve.wait_ge(stats_ready, 2 * i - 1 + k_unit)
                aggregation_rest(u, 1)
                if normed:
                    moments(parity)
                if not ended:
                    dve.wait_ge(ht_head_ready, u + 2)
                    rest(ht_rest[:, other, :, :], ht[:, other, :, :], ht_head[:, other, :, :]
                         ).then_inc(ht_rest_ready, 1)
                elif following:
                    split_x_t(pair, other)
                    split_x(pair, other)
                h = state(k_unit)
                for k in range(K):
                    dve.wait_ge(r_ready, 2 * u + k + 1)
                    nc.vector.tensor_tensor(rh[:, k, :], r[:, k, :], h[:, k, :], ALU.mult).then_inc(rh_ready, 1)
                for k in range(K):
                    dve.wait_ge(rh_head_ready, 2 * u + k + 1)
                    rest(rh_rest[:, k, :], rh[:, k, :], rh_head[:, k, :]).then_inc(rh_rest_ready, 1)
                if normed:
                    normalise(i - 1, parity)
                dve.wait_ge(z_done, u + 1)
                dve.wait_ge(u3_copied, 2 * u + 2)
                nc.vector.tensor_tensor(z[:, :, :], ps_z[:, :, :], u3h[:, :, :], ALU.add).then_inc(z_summed, 1)
                if not ended:
                    split_hn(u, other)
                elif not very_first:
                    residual(u, i if k_unit else i - 1, other)
            split_x(0, 0)
            for c in range(C):
                dve.wait_ge(adj_head_ready, c + 1)
                rest(adj_rest[:, c, :], adj_raw[:, c, :], adj_head[:, c, :]).then_inc(adj_rest_ready, 1)
            split_x_t(0, 0)
            dve.wait_ge(bias_landed, 16)
            for n, (b, c) in enumerate(((0, 1), (2, 1), (3, 4))):
                nc.vector.tensor_tensor(bias[:, n, :], bias_raw[:, b, :], bias_raw[:, c, :], ALU.add
                                        ).then_inc(bias_ready, 1)
            for n, w in enumerate(names):
                if halves[w] == 2:
                    dve.wait_ge(w_landed[w], 16)
                    nc.vector.tensor_tensor(w_raw[w][:, 0, :, :], w_raw[w][:, 0, :, :], w_raw[w][:, 1, :, :],
                                            ALU.add).then_inc(w_summed, 1)
                dve.wait_ge(w_head_ready, n + 1)
                rest(w_rest[w][:, :, :], w_raw[w][:, 0, :, :], w_head[w][:, :, :]).then_inc(w_rest_ready, 1)

            for k_unit in range(UNITS):
                unit(0, k_unit)
            with dve.Fori(1, PAIRS - 1) as i:
                for k_unit in range(UNITS):
                    unit(i, k_unit)
            for k_unit in range(UNITS):
                unit(PAIRS - 1, k_unit, last_pair=True)
            units = UNITS * PAIRS
            new_state(units, state(UNITS - 1), 1)
            transpose_blocks(units, 1)
            dve.wait_ge(y_ready, B - 1)
            statistics(PAIRS - 1, 0)
            dve.wait_ge(stats_ready, B - 1)
            moments(0)
            normalise(PAIRS - 1, 0)
            residual(units, PAIRS - 1, 1)
            dve.wait_ge(y_ready, B)
            statistics(PAIRS - 1, 1)
            dve.wait_ge(stats_ready, B)
            moments(1)
            normalise(PAIRS - 1, 1)


def kernel(x, adj, L0_gnn_w3_w, L0_gnn_w3_b, L0_gnn_u3_w, L0_gnn_u3_b, L0_gnn_w4_w, L0_gnn_w4_b,
           L0_gnn_w5_w, L0_gnn_w5_b, L0_gnn_u5_w, L0_gnn_u5_b):
    import numpy as np
    import concourse.bacc as bacc
    from concourse.bass_utils import run_bass_kernel_spmd

    B, N, D = x.shape
    C, K, Q, E = N // P, D // P, P // 32, 32
    x, adj = np.asarray(x), np.asarray(adj)

    def weights(w):
        w = np.asarray(w)
        return np.ascontiguousarray(w.T.reshape(-1, P, D).transpose(1, 0, 2).reshape(P, -1))

    def aggregation_weights(w):
        w = np.asarray(w)
        return weights(w.reshape(D, -1, K, Q, E).transpose(0, 1, 3, 2, 4).reshape(D, -1))

    arrays = {
        "x": np.ascontiguousarray(x.reshape(B, P, C, K, Q, E).transpose(0, 1, 4, 3, 2, 5).reshape(B, P, -1)),
        "x_t": np.ascontiguousarray(x.reshape(B, P, C, D).transpose(0, 3, 2, 1).reshape(B, D, N)),
        "adj_t": np.ascontiguousarray(adj.reshape(P, C, N).transpose(2, 1, 0).reshape(N, N)),
        "u3_t": weights(L0_gnn_u3_w),
        "w4_t": aggregation_weights(L0_gnn_w4_w),
        "w3_t": aggregation_weights(L0_gnn_w3_w),
        "w5_t": aggregation_weights(L0_gnn_w5_w),
        "u5_t": weights(L0_gnn_u5_w),
        "biases": np.ascontiguousarray(
            np.stack([np.asarray(b) for b in (L0_gnn_w3_b, L0_gnn_u3_b, L0_gnn_w4_b, L0_gnn_w5_b, L0_gnn_u5_b)])
            .reshape(5, D // P, P).transpose(2, 0, 1).reshape(P, -1)),
    }
    nc = bacc.Bacc("TRN2", target_bir_lowering=False, num_devices=1)
    args = [nc.dram_tensor(f"in_{n}", a.shape, F32, kind="ExternalInput").ap() for n, a in arrays.items()]
    args.append(nc.dram_tensor("out", (B, P, C * D), F32, kind="ExternalOutput").ap())
    gated_graph_resnorm(nc, B, N, D, *args)
    result = run_bass_kernel_spmd(nc, [{f"in_{n}": a for n, a in arrays.items()}], core_ids=[0])
    out = result.results[0]["out"].reshape(B, P, Q, K, C, E)
    return np.ascontiguousarray(out.transpose(0, 1, 4, 3, 2, 5).reshape(B, N, D))
```

```python
from contextlib import ExitStack

import concourse.bass as bass
from concourse import mybir

P = 128
F32 = mybir.dt.float32
F32R = mybir.dt.float32r
ALU = mybir.AluOpType
ACT = mybir.ActivationFunctionType

STEPS = 3
EPS = 1e-5
WARM_PRODUCTS = 9


def gated_graph_resnorm(nc, B, N, D, x, x_t, adj_t, u3_t, w4_t, w3_t, w5_t, u5_t, biases, out):
    C = N // P
    K = D // P
    PAIRS = B // 2
    UNITS = 2 * STEPS
    Q = P // 32
    E = 32
    QF = C * D // Q
    assert N == 512 and K == 2 and C * D == K * N

    with ExitStack() as ctx:
        def sb(name, shape, dt=F32):
            return ctx.enter_context(nc.sbuf_tensor(name, shape, dt))

        def sem(name):
            return ctx.enter_context(nc.semaphore(name))

        ps_agg = ctx.enter_context(nc.psum_tensor("ps_agg", [P, K, N], F32))
        ps_r = ctx.enter_context(nc.psum_tensor("ps_r", [P, K, N], F32))
        ps_z = ctx.enter_context(nc.psum_tensor("ps_z", [P, K, N], F32))
        ps_v = ctx.enter_context(nc.psum_tensor("ps_v", [P, K, N], F32))

        ps_turned = [t[:, k, 0:D] for t in (ps_agg, ps_z) for k in range(K)]
        assert len(ps_turned) == C

        x_all = sb("x_all", [P, B, C * D])
        xt = sb("xt", [P, 2, K, N])
        adj_raw = x_all[:, B - 2:B, :].rearrange("p b f -> p (b f)").rearrange("p (c n) -> p c n", n=N)
        names = ["u3", "w4", "w3", "w5", "u5"]
        halves = {"u3": 1, "w4": 2, "w3": 2, "w5": 2, "u5": 1}
        w_dram = {"u3": u3_t, "w4": w4_t, "w3": w3_t, "w5": w5_t, "u5": u5_t}
        w_raw = {w: x_all[:, B - 3 - n, 0:halves[w] * K * D].rearrange("p (a k d) -> p a k d", k=K, d=D)
                 for n, w in enumerate(names)}
        bias_raw = sb("bias_raw", [P, 5, K])
        bias = sb("bias", [P, 3, K])
        identity = sb("identity", [P, P])

        adj_head, adj_rest = sb("adj_head", [P, C, N], F32R), sb("adj_rest", [P, C, N], F32R)
        w_head = {w: sb(f"{w}_head", [P, K, D], F32R) for w in names}
        w_rest = {w: sb(f"{w}_rest", [P, K, D], F32R) for w in names}
        hn_head, hn_rest = (sb(n, [P, 2, C, D], F32R) for n in ("hn_head", "hn_rest"))
        ht_head, ht_rest = (sb(n, [P, 2, K, N], F32R) for n in ("ht_head", "ht_rest"))
        a_head, a_rest = (sb(n, [P, K, N], F32R) for n in ("a_head", "a_rest"))
        rh_head, rh_rest = (sb(n, [P, K, N], F32R) for n in ("rh_head", "rh_rest"))

        ht = sb("ht", [P, 2, K, N])
        h_blocks = sb("h_blocks", [P, Q, K * C * E])
        hn = sb("hn", [P, Q, QF])
        u3h = sb("u3h", [P, K, N])
        r = sb("r", [P, K, N])
        rh = sb("rh", [P, K, N])
        z = sb("z", [P, K, N])
        v = sb("v", [P, K, N])

        stats = sb("stats", [P, 2, C, 6])
        mean_var = sb("mean_var", [P, 2, C, 2])
        var_eps = sb("var_eps", [P, 2, C])
        eps = sb("eps", [P, C])
        minus_half = sb("minus_half", [P, C])
        rstd = sb("rstd", [P, 2, C])
        zero = sb("zero", [P, 1])
        table_use = sb("table_use", [P, 1])

        x_landed = [sem("x_even_landed"), sem("x_odd_landed")]
        xt_landed = [sem("xt_even_landed"), sem("xt_odd_landed")]
        adj_landed = [sem(f"adj{c}_landed") for c in range(C)]
        w_landed = {w: sem(f"{w}_landed") for w in names}
        bias_landed = sem("bias_landed")
        out_stored = sem("out_stored")
        constants_set = sem("constants_set")
        identity_ready = sem("identity_ready")
        warm_ready = sem("warm_ready")
        zero_ready = sem("zero_ready")
        turned = sem("turned")
        bias_ready = sem("bias_ready")
        adj_head_ready = sem("adj_head_ready")
        adj_rest_ready = sem("adj_rest_ready")
        w_summed = sem("w_summed")
        w_head_ready = sem("w_head_ready")
        w_rest_ready = sem("w_rest_ready")
        hn_head_ready = sem("hn_head_ready")
        hn_rest_ready = sem("hn_rest_ready")
        ht_head_ready = sem("ht_head_ready")
        ht_rest_ready = sem("ht_rest_ready")
        agg_done = sem("agg_done")
        u3_done = sem("u3_done")
        r_done = sem("r_done")
        z_done = sem("z_done")
        v_done = sem("v_done")
        a_head_ready = sem("a_head_ready")
        a_rest_ready = sem("a_rest_ready")
        u3_copied = sem("u3_copied")
        r_ready = sem("r_ready")
        rh_ready = sem("rh_ready")
        rh_head_ready = sem("rh_head_ready")
        rh_rest_ready = sem("rh_rest_ready")
        z_summed = sem("z_summed")
        z_ready = sem("z_ready")
        v_ready = sem("v_ready")
        v_minus_h = sem("v_minus_h")
        v_times_z = sem("v_times_z")
        h_ready = sem("h_ready")
        blocks_ready = sem("blocks_ready")
        hn_moved = sem("hn_moved")
        y_ready = sem("y_ready")
        stats_ready = sem("stats_ready")
        moments_ready = sem("moments_ready")
        eps_added = sem("eps_added")
        rstd_ready = sem("rstd_ready")
        out_ready = sem("out_ready")

        xt_dram = x_t.rearrange("b (k p) n -> b p k n", p=P)
        adj_dram = adj_t.rearrange("(p c) n -> p c n", c=C)

        block = ctx.enter_context(nc.Block())

        @block.sync
        def _(sp):
            def load_x(pair, parity):
                sp.dma_start(x_all[:, bass.ds(2 * pair + parity, 1), :],
                             x[bass.ds(2 * pair + parity, 1), :, :].rearrange("b p f -> p b f"),
                             ).then_inc(x_landed[parity], 16)

            def load_xt(pair, parity):
                sp.dma_start(xt[:, parity, :, :],
                             xt_dram[bass.ds(2 * pair + parity, 1), :, :, :].rearrange("b p k n -> p (b k) n"),
                             ).then_inc(xt_landed[parity], 16)

            def store(pair, parity):
                sp.wait_ge(out_ready, 2 * pair + parity + 1)
                sp.dma_start(out[bass.ds(2 * pair + parity, 1), :, :].rearrange("b p f -> p b f"),
                             x_all[:, bass.ds(2 * pair + parity, 1), :],
                             ).then_inc(out_stored, 16)

            def load_next(pair):
                for parity in range(2):
                    sp.wait_ge(x_landed[parity], 16 * (pair + 1))
                    load_x(pair + 1, parity)
                    sp.wait_ge(h_ready, 2 * (UNITS * pair + parity + 1))
                    load_xt(pair + 1, parity)

            for c in range(C):
                sp.dma_start(adj_raw[:, c, :], adj_dram[:, c, :]).then_inc(adj_landed[c], 16)
                if c == 0:
                    load_x(0, 0)
            load_xt(0, 0)
            for w in names:
                sp.dma_start(w_raw[w].rearrange("p a k d -> p (a k d)"), w_dram[w]
                             ).then_inc(w_landed[w], 16)
                if w == "u3":
                    sp.dma_start(bias_raw[:, :, :].rearrange("p b k -> p (b k)"), biases
                                 ).then_inc(bias_landed, 16)
            load_x(0, 1)
            load_xt(0, 1)

            load_next(0)
            with sp.Fori(1, PAIRS - 1) as pair:
                store(pair - 1, 0)
                store(pair - 1, 1)
                load_next(pair)
            for pair in (PAIRS - 2, PAIRS - 1):
                store(pair, 0)
                store(pair, 1)
            sp.wait_ge(out_stored, 16 * B)

        @block.gpsimd
        def _(pool):
            nc.gpsimd.memset(identity[:, :], 0.0).then_inc(constants_set, 1)
            nc.gpsimd.memset(minus_half[:, :], -0.5).then_inc(constants_set, 1)
            nc.gpsimd.memset(eps[:, :], EPS).then_inc(constants_set, 1)
            pool.wait_ge(constants_set, 3)
            nc.gpsimd.affine_select(out=identity[:, :], in_=identity[:, :], compare_op=ALU.not_equal,
                                    fill=1.0, base=0, pattern=[[-1, P]], channel_multiplier=1
                                    ).then_inc(identity_ready, 1)

            def inverse_deviation(graph, parity):
                pool.wait_ge(moments_ready, graph + 1)
                nc.gpsimd.tensor_tensor(var_eps[:, parity, :], mean_var[:, parity, :, 1], eps[:, :], ALU.add
                                        ).then_inc(eps_added, 1)
                pool.wait_ge(eps_added, graph + 1)
                nc.gpsimd.tensor_tensor(rstd[:, parity, :], var_eps[:, parity, :], minus_half[:, :], ALU.pow
                                        ).then_inc(rstd_ready, 1)

            with pool.Fori(0, PAIRS) as pair:
                inverse_deviation(2 * pair, 0)
                inverse_deviation(2 * pair + 1, 1)

        @block.tensor
        def _(pe):
            def product(acc, lhs_head, lhs_rest, rhs_head, rhs_rest, first, last=False, joins=False):
                nc.tensor.matmul(acc, lhs_head, rhs_head, start=first, stop=False, skip_group_check=joins)
                nc.tensor.matmul(acc, lhs_head, rhs_rest, start=False, stop=False, skip_group_check=joins)
                return nc.tensor.matmul(acc, lhs_rest, rhs_head, start=False, stop=last, skip_group_check=joins)

            def aggregate(parity, k, c, state, adjacency):
                return nc.tensor.matmul(ps_agg[:, k, :], state[:, parity, c, k * P:(k + 1) * P], adjacency[:, c, :],
                                        start=c == 0 and state is hn_head and adjacency is adj_head,
                                        stop=c == C - 1 and state is hn_rest)

            def weigh(w, acc, head, rest, k, o, first=False, last=False, joins=False):
                cols = slice(o * P, (o + 1) * P)
                return product(acc[:, o, :], w_head[w][:, k, cols], w_rest[w][:, k, cols],
                               head[:, k, :], rest[:, k, :], first, last, joins)

            def unit(i, k_unit):
                u = UNITS * i + k_unit
                parity = k_unit % 2
                first_pair = isinstance(i, int) and i == 0
                setup = very_first = first_pair and k_unit == 0

                pe.wait_ge(hn_head_ready, u + 1)
                if setup:
                    for c in range(C):
                        pe.wait_ge(adj_head_ready, c + 1)
                        for k in range(K):
                            aggregate(parity, k, c, hn_head, adj_head)
                        pe.wait_ge(adj_rest_ready, c + 1)
                        for k in range(K):
                            aggregate(parity, k, c, hn_head, adj_rest)
                for k in range(K):
                    if not setup:
                        for c in range(C):
                            aggregate(parity, k, c, hn_head, adj_head)
                            aggregate(parity, k, c, hn_head, adj_rest)
                    if k == 0:
                        pe.wait_ge(hn_rest_ready, u + 1)
                    for c in range(C):
                        last = aggregate(parity, k, c, hn_rest, adj_head)
                    last.then_inc(agg_done, 1)

                pe.wait_ge(ht_head_ready, u + 1)
                pe.wait_ge(ht_rest_ready, u + 1)
                if setup:
                    pe.wait_ge(w_head_ready, 1)
                    pe.wait_ge(w_rest_ready, 1)
                else:
                    pe.wait_ge(r_ready, 2 * u)
                for o in range(K):
                    for k in range(K):
                        last = weigh("u3", ps_r, ht_head[:, parity], ht_rest[:, parity], k, o,
                                     first=k == 0, last=k == K - 1)
                    last.then_inc(u3_done, 1)

                if setup:
                    pe.wait_ge(w_head_ready, 2)
                    pe.wait_ge(w_rest_ready, 2)
                for o in range(K):
                    pe.wait_ge(u3_copied, 2 * u + o + 1)
                    for k in range(K):
                        if o == 0:
                            pe.wait_ge(a_head_ready, 2 * u + k + 1)
                            pe.wait_ge(a_rest_ready, 2 * u + k + 1)
                        last = weigh("w4", ps_r, a_head, a_rest, k, o, last=k == K - 1, joins=True)
                    last.then_inc(r_done, 1)

                if setup:
                    pe.wait_ge(w_head_ready, 3)
                    pe.wait_ge(w_rest_ready, 3)
                else:
                    pe.wait_ge(z_summed, u)
                for o in range(K):
                    for k in range(K):
                        last = weigh("w3", ps_z, a_head, a_rest, k, o, first=k == 0, last=k == K - 1)
                last.then_inc(z_done, 1)

                if setup:
                    pe.wait_ge(w_head_ready, 4)
                    pe.wait_ge(w_rest_ready, 4)
                else:
                    pe.wait_ge(v_ready, 2 * u)
                for o in range(K):
                    for k in range(K):
                        weigh("w5", ps_v, a_head, a_rest, k, o, first=k == 0)
                if setup:
                    pe.wait_ge(w_head_ready, 5)
                    pe.wait_ge(w_rest_ready, 5)
                for o in range(K):
                    for k in range(K):
                        if o == 0:
                            pe.wait_ge(rh_head_ready, 2 * u + k + 1)
                            pe.wait_ge(rh_rest_ready, 2 * u + k + 1)
                        last = weigh("u5", ps_v, rh_head, rh_rest, k, o, last=k == K - 1)
                    last.then_inc(v_done, 1)

            pe.wait_ge(warm_ready, 1)
            for _ in range(WARM_PRODUCTS):
                nc.tensor.matmul(ps_v[:, 0, :], a_head[:, 0, 0:P], a_head[:, 0, :], start=True, stop=True)

            for k_unit in range(UNITS):
                unit(0, k_unit)
            with pe.Fori(1, PAIRS) as i:
                for k_unit in range(UNITS):
                    unit(i, k_unit)

            pe.wait_ge(identity_ready, 1)
            pe.wait_ge(h_ready, 2 * UNITS * PAIRS)
            for c in range(C):
                for k in range(K):
                    last = nc.tensor.transpose(ps_turned[c][:, k * P:(k + 1) * P], ht[:, 1, k, c * P:(c + 1) * P],
                                               identity[:, :])
                last.then_inc(turned, 1)

        @block.scalar
        def _(act):
            def weight_head(w):
                n = names.index(w)
                if halves[w] == 2:
                    act.wait_ge(w_summed, n)
                else:
                    act.wait_ge(w_landed[w], 16)
                nc.scalar.copy(w_head[w][:, :, :], w_raw[w][:, 0, :, :]).then_inc(w_head_ready, 1)

            def candidate(u):
                for o in range(K):
                    act.wait_ge(v_done, 2 * u - 1 + o)
                    nc.scalar.activation(v[:, o, :], ps_v[:, o, :], ACT.Tanh, bias=bias[:, 2, o:o + 1]
                                         ).then_inc(v_ready, 1)

            def aggregation_head(u, k):
                act.wait_ge(agg_done, 2 * u + k + 1)
                nc.scalar.copy(a_head[:, k, :], ps_agg[:, k, :]).then_inc(a_head_ready, 1)

            def split_x_t(pair, parity):
                act.wait_ge(xt_landed[parity], 16 * (pair + 1))
                nc.scalar.copy(ht_head[:, parity, :, :], xt[:, parity, :, :]).then_inc(ht_head_ready, 1)

            def move(n, count):
                for m in range(n, n + count):
                    q, j = m // Q, m % Q
                    last = nc.scalar.copy(hn[E * j:E * (j + 1), q, :], h_blocks[E * q:E * (q + 1), j, :])
                if n + count == Q * Q:
                    last.then_inc(hn_moved, 1)

            def unit(i, k_unit, last_pair=False):
                u = UNITS * i + k_unit
                other = 1 - k_unit % 2
                very_first = isinstance(i, int) and i == 0 and k_unit == 0
                ended = k_unit in (0, UNITS - 1)
                following = not (last_pair and k_unit == UNITS - 1)
                pair = i if k_unit == 0 else i + 1

                if not very_first:
                    candidate(u)
                aggregation_head(u, 0)
                if not ended:
                    act.wait_ge(h_ready, 2 * u)
                    nc.scalar.copy(ht_head[:, other, :, :], ht[:, other, :, :]).then_inc(ht_head_ready, 1)
                elif following and not very_first:
                    split_x_t(pair, other)
                aggregation_head(u, 1)
                if not very_first:
                    act.wait_ge(blocks_ready, u)
                    move(0, 2)
                for o in range(K):
                    act.wait_ge(u3_done, 2 * u + o + 1)
                    nc.scalar.copy(u3h[:, o, :], ps_r[:, o, :]).then_inc(u3_copied, 1)
                    if not very_first:
                        move(2 + 3 * o, 3)
                if very_first:
                    weight_head("w3")
                for o in range(K):
                    act.wait_ge(r_done, 2 * u + o + 1)
                    nc.scalar.activation(r[:, o, :], ps_r[:, o, :], ACT.Sigmoid, bias=bias[:, 1, o:o + 1]
                                         ).then_inc(r_ready, 1)
                    if very_first and o == 0:
                        weight_head("w5")
                    elif o == 0:
                        move(8, 2)
                for k in range(K):
                    act.wait_ge(rh_ready, 2 * u + k + 1)
                    nc.scalar.copy(rh_head[:, k, :], rh[:, k, :]).then_inc(rh_head_ready, 1)
                if very_first:
                    weight_head("u5")
                if not very_first:
                    move(10, 6)
                else:
                    split_x_t(pair, other)
                act.wait_ge(z_summed, u + 1)
                for o in range(K):
                    nc.scalar.activation(z[:, o, :], z[:, o, :], ACT.Sigmoid, bias=bias[:, 0, o:o + 1]
                                         ).then_inc(z_ready, 1)

            act.wait_ge(zero_ready, 1)
            nc.scalar.activation(table_use[:, :], zero[:, :], ACT.Sigmoid)
            for c in range(C):
                act.wait_ge(adj_landed[c], 16)
                nc.scalar.copy(adj_head[:, c, :], adj_raw[:, c, :]).then_inc(adj_head_ready, 1)
            split_x_t(0, 0)
            weight_head("u3")
            weight_head("w4")
            act.wait_ge(bias_ready, 3)

            for k_unit in range(UNITS):
                unit(0, k_unit)
            with act.Fori(1, PAIRS - 1) as i:
                for k_unit in range(UNITS):
                    unit(i, k_unit)
            for k_unit in range(UNITS):
                unit(PAIRS - 1, k_unit, last_pair=True)
            candidate(UNITS * PAIRS)

        @block.vector
        def _(dve):
            def rest(out_, whole, head):
                return nc.vector.tensor_tensor(out_, whole, head.bitcast(F32), ALU.subtract)

            def aggregation_rest(u, k):
                dve.wait_ge(a_head_ready, 2 * u + k + 1)
                rest(a_rest[:, k, :], ps_agg[:, k, :], a_head[:, k, :]).then_inc(a_rest_ready, 1)

            def split_x_t(pair, parity):
                dve.wait_ge(ht_head_ready, UNITS * pair + parity + 1)
                rest(ht_rest[:, parity, :, :], xt[:, parity, :, :], ht_head[:, parity, :, :]
                     ).then_inc(ht_rest_ready, 1)

            def by_chunk(t, parity):
                return t[:, parity, :, :].rearrange("p c (f e) -> p f c e", e=E)

            def nodes_head(whole, parity):
                nc.vector.tensor_scalar(by_chunk(hn_head, parity), whole, 1.0, None, ALU.mult
                                        ).then_inc(hn_head_ready, 1)

            def nodes_rest(whole, parity, n):
                dve.wait_ge(hn_head_ready, n)
                rest(by_chunk(hn_rest, parity), whole, by_chunk(hn_head, parity)).then_inc(hn_rest_ready, 1)

            def as_rows(whole):
                return whole.rearrange("p (f c e) -> p f c e", c=C, e=E)

            def x_head(pair, parity):
                dve.wait_ge(x_landed[parity], 16 * (pair + 1))
                nodes_head(as_rows(rows(pair, parity)), parity)

            def x_rest(pair, parity):
                nodes_rest(as_rows(rows(pair, parity)), parity, UNITS * pair + parity + 1)

            def split_hn(u, parity):
                whole = as_rows(hn[:, :, :].rearrange("p q f -> p (q f)"))
                dve.wait_ge(hn_moved, u)
                nodes_head(whole, parity)
                nodes_rest(whole, parity, u + 2)

            def adjacency_rest(c):
                dve.wait_ge(adj_head_ready, c + 1)
                rest(adj_rest[:, c, :], adj_raw[:, c, :], adj_head[:, c, :]).then_inc(adj_rest_ready, 1)

            def weight_sum(w):
                dve.wait_ge(w_landed[w], 16)
                nc.vector.tensor_tensor(w_raw[w][:, 0, :, :], w_raw[w][:, 0, :, :], w_raw[w][:, 1, :, :],
                                        ALU.add).then_inc(w_summed, 1)

            def weight_rest(w):
                n = names.index(w)
                dve.wait_ge(w_head_ready, n + 1)
                rest(w_rest[w][:, :, :], w_raw[w][:, 0, :, :], w_head[w][:, :, :]).then_inc(w_rest_ready, 1)

            def less_state(u, o, h):
                dve.wait_ge(v_ready, 2 * u - 1 + o)
                nc.vector.tensor_tensor(v[:, o, :], v[:, o, :], h[:, o, :], ALU.subtract).then_inc(v_minus_h, 1)

            def times_z(u, o):
                dve.wait_ge(v_minus_h, 2 * u - 1 + o)
                dve.wait_ge(z_ready, 2 * u - 1 + o)
                nc.vector.tensor_tensor(v[:, o, :], v[:, o, :], z[:, o, :], ALU.mult).then_inc(v_times_z, 1)

            def plus_state(u, o, h, parity):
                dve.wait_ge(v_times_z, 2 * u - 1 + o)
                nc.vector.tensor_tensor(ht[:, parity, o, :], v[:, o, :], h[:, o, :], ALU.add).then_inc(h_ready, 1)

            def new_state(u, h, parity):
                less_state(u, 0, h)
                times_z(u, 0)
                less_state(u, 1, h)
                plus_state(u, 0, h, parity)
                times_z(u, 1)
                plus_state(u, 1, h, parity)

            def transpose_blocks(u, parity):
                dve.wait_ge(h_ready, 2 * u)
                nc.vector.transpose(h_blocks[:, :, :].rearrange("p j (f e) -> p j f e", e=E),
                                    ht[:, parity, :, :].rearrange("p k n -> p (k n)")
                                    .rearrange("p (f j i) -> p j f i", j=Q, i=E)).then_inc(blocks_ready, 1)

            def rows(pair, parity):
                return x_all[:, bass.ds(2 * pair + parity, 1), :].rearrange("p b f -> p (b f)")

            def chunk(y, c):
                return y.rearrange("p (f c e) -> p f c e", c=C, e=E)[:, :, c, :]

            def residual(u, pair, parity):
                y = rows(pair, parity)
                dve.wait_ge(hn_moved, u)
                nc.vector.tensor_tensor(y, hn[:, :, :].rearrange("p q f -> p (q f)"), y, ALU.add).then_inc(y_ready, 1)

            def statistics(pair, parity):
                y = rows(pair, parity)
                for c in range(C):
                    last = nc.vector.bn_stats(stats[:, parity, c, :], chunk(y, c))
                last.then_inc(stats_ready, 1)

            def moments(parity):
                for c in range(C):
                    last = nc.vector.bn_aggr(mean_var[:, parity, c, :], stats[:, parity, c, :])
                last.then_inc(moments_ready, 1)

            def normalise(pair, parity):
                y = rows(pair, parity)
                dve.wait_ge(rstd_ready, 2 * pair + parity + 1)
                for c in range(C):
                    last = nc.vector.tensor_scalar(chunk(y, c), chunk(y, c), mean_var[:, parity, c, 0:1],
                                                   rstd[:, parity, c:c + 1], ALU.subtract, ALU.mult)
                last.then_inc(out_ready, 1)

            def state(k_unit):
                return xt[:, k_unit % 2, :, :] if k_unit < 2 else ht[:, k_unit % 2, :, :]

            def unit(i, k_unit, last_pair=False):
                u = UNITS * i + k_unit
                parity, other = k_unit % 2, 1 - k_unit % 2
                first_pair = isinstance(i, int) and i == 0
                very_first = first_pair and k_unit == 0
                ended = k_unit in (0, UNITS - 1)
                following = not (last_pair and k_unit == UNITS - 1)
                pair = i if k_unit == 0 else i + 1
                h_before = state((k_unit - 1) % UNITS)
                normed = k_unit < 2 and not first_pair

                if not very_first:
                    new_state(u, h_before, other)
                aggregation_rest(u, 0)
                if not very_first:
                    transpose_blocks(u, other)
                if normed:
                    dve.wait_ge(y_ready, 2 * i - 1 + k_unit)
                aggregation_rest(u, 1)
                if normed:
                    statistics(i - 1, parity)
                    dve.wait_ge(stats_ready, 2 * i - 1 + k_unit)
                if not ended:
                    dve.wait_ge(ht_head_ready, u + 2)
                    rest(ht_rest[:, other, :, :], ht[:, other, :, :], ht_head[:, other, :, :]
                         ).then_inc(ht_rest_ready, 1)
                elif following and not very_first:
                    split_x_t(pair, other)
                if very_first:
                    weight_sum("w3")
                    weight_rest("w3")
                    weight_sum("w5")
                if normed:
                    moments(parity)
                if ended and following and not very_first:
                    x_head(pair, other)
                    x_rest(pair, other)
                h = state(k_unit)
                for k in range(K):
                    dve.wait_ge(r_ready, 2 * u + k + 1)
                    nc.vector.tensor_tensor(rh[:, k, :], r[:, k, :], h[:, k, :], ALU.mult).then_inc(rh_ready, 1)
                    if very_first and k == 0:
                        weight_rest("w5")
                for k in range(K):
                    dve.wait_ge(rh_head_ready, 2 * u + k + 1)
                    rest(rh_rest[:, k, :], rh[:, k, :], rh_head[:, k, :]).then_inc(rh_rest_ready, 1)
                if very_first:
                    weight_rest("u5")
                if normed:
                    normalise(i - 1, parity)
                dve.wait_ge(z_done, u + 1)
                dve.wait_ge(u3_copied, 2 * u + 2)
                nc.vector.tensor_tensor(z[:, :, :], ps_z[:, :, :], u3h[:, :, :], ALU.add).then_inc(z_summed, 1)
                if not ended:
                    split_hn(u, other)
                elif very_first:
                    x_head(pair, other)
                    x_rest(pair, other)
                    split_x_t(pair, other)
                else:
                    residual(u, i if k_unit else i - 1, other)
            nc.vector.memset(zero[:, :], 0.0).then_inc(zero_ready, 1)
            nc.vector.memset(a_head[:, 0, :].bitcast(mybir.dt.uint32), 0).then_inc(warm_ready, 1)
            adjacency_rest(0)
            x_head(0, 0)
            for c in range(1, C):
                adjacency_rest(c)
            x_rest(0, 0)
            split_x_t(0, 0)
            dve.wait_ge(bias_landed, 16)
            for n, (b, c) in enumerate(((0, 1), (2, 1), (3, 4))):
                nc.vector.tensor_tensor(bias[:, n, :], bias_raw[:, b, :], bias_raw[:, c, :], ALU.add
                                        ).then_inc(bias_ready, 1)
            weight_rest("u3")
            weight_sum("w4")
            weight_rest("w4")

            for k_unit in range(UNITS):
                unit(0, k_unit)
            with dve.Fori(1, PAIRS - 1) as i:
                for k_unit in range(UNITS):
                    unit(i, k_unit)
            for k_unit in range(UNITS):
                unit(PAIRS - 1, k_unit, last_pair=True)
            units = UNITS * PAIRS
            dve.wait_ge(y_ready, B - 1)
            statistics(PAIRS - 1, 0)
            new_state(units, state(UNITS - 1), 1)
            dve.wait_ge(stats_ready, B - 1)
            moments(0)
            y = rows(PAIRS - 1, 1)
            for c in range(C):
                dve.wait_ge(turned, c + 1)
                by_quadrant = [t.rearrange(how, q=Q, k=K) for t, how in (
                    (ps_turned[c], "p (k q e) -> p q k e"), (chunk(y, c), "p (q k) e -> p q k e"))]
                nc.vector.tensor_tensor(by_quadrant[1], by_quadrant[0], by_quadrant[1], ALU.add).then_inc(y_ready, 1)
            dve.wait_ge(y_ready, B - 1 + C)
            statistics(PAIRS - 1, 1)
            dve.wait_ge(stats_ready, B)
            moments(1)
            normalise(PAIRS - 1, 0)
            normalise(PAIRS - 1, 1)


def kernel(x, adj, L0_gnn_w3_w, L0_gnn_w3_b, L0_gnn_u3_w, L0_gnn_u3_b, L0_gnn_w4_w, L0_gnn_w4_b,
           L0_gnn_w5_w, L0_gnn_w5_b, L0_gnn_u5_w, L0_gnn_u5_b):
    import numpy as np
    import concourse.bacc as bacc
    from concourse.bass_utils import run_bass_kernel_spmd

    B, N, D = x.shape
    C, K, Q, E = N // P, D // P, P // 32, 32
    x, adj = np.asarray(x), np.asarray(adj)

    def weights(w):
        w = np.asarray(w)
        return np.ascontiguousarray(w.T.reshape(-1, P, D).transpose(1, 0, 2).reshape(P, -1))

    def aggregation_weights(w):
        w = np.asarray(w)
        return weights(w.reshape(D, -1, K, Q, E).transpose(0, 1, 3, 2, 4).reshape(D, -1))

    arrays = {
        "x": np.ascontiguousarray(x.reshape(B, P, C, K, Q, E).transpose(0, 1, 4, 3, 2, 5).reshape(B, P, -1)),
        "x_t": np.ascontiguousarray(x.reshape(B, P, C, D).transpose(0, 3, 2, 1).reshape(B, D, N)),
        "adj_t": np.ascontiguousarray(adj.reshape(P, C, N).transpose(2, 1, 0).reshape(N, N)),
        "u3_t": weights(L0_gnn_u3_w),
        "w4_t": aggregation_weights(L0_gnn_w4_w),
        "w3_t": aggregation_weights(L0_gnn_w3_w),
        "w5_t": aggregation_weights(L0_gnn_w5_w),
        "u5_t": weights(L0_gnn_u5_w),
        "biases": np.ascontiguousarray(
            np.stack([np.asarray(b) for b in (L0_gnn_w3_b, L0_gnn_u3_b, L0_gnn_w4_b, L0_gnn_w5_b, L0_gnn_u5_b)])
            .reshape(5, D // P, P).transpose(2, 0, 1).reshape(P, -1)),
    }
    nc = bacc.Bacc("TRN2", target_bir_lowering=False, num_devices=1)
    args = [nc.dram_tensor(f"in_{n}", a.shape, F32, kind="ExternalInput").ap() for n, a in arrays.items()]
    args.append(nc.dram_tensor("out", (B, P, C * D), F32, kind="ExternalOutput").ap())
    gated_graph_resnorm(nc, B, N, D, *args)
    result = run_bass_kernel_spmd(nc, [{f"in_{n}": a for n, a in arrays.items()}], core_ids=[0])
    out = result.results[0]["out"].reshape(B, P, Q, K, C, E)
    return np.ascontiguousarray(out.transpose(0, 1, 4, 3, 2, 5).reshape(B, N, D))
```
